# Optimizing a Trainium2 kernel written in Bass

```python
import numpy as np
import jax
import jax.numpy as jnp

def _softmax(x, axis=-1):
    return jax.nn.softmax(x, axis=axis)

def _gelu(x):
    return jax.nn.gelu(x, approximate=True)

def _silu(x):
    return jax.nn.silu(x)

def _sigmoid(x):
    return jax.nn.sigmoid(x)

def _layernorm(x, axis=-1, eps=1e-05):
    m = jnp.mean(x, axis=axis, keepdims=True)
    v = jnp.var(x, axis=axis, keepdims=True)
    return (x - m) / jnp.sqrt(v + eps)

def _scatter_add(tgt, idx, src, axis=0):
    return tgt.at[idx].add(src)

def _segment_sum(src, seg, n):
    return jax.ops.segment_sum(src, seg, n)
kernel_name = 'mk_dlrm_tower_d1_rec_r8_5e5980'

def setup_inputs(seed: int=0):
    np.random.seed(seed)
    _w = jnp.asarray

    def _rec_inputs():
        import jax
        import jax.numpy as jnp
        _tk = jax.random.key(seed)
        ids = jnp.stack([jax.random.randint(jax.random.fold_in(_tk, 200 + f), (2048,), 0, v, jnp.int32) for f, v in enumerate([1000, 1250, 12500, 125000, 1000, 1000, 12500, 1250, 1000, 12500, 12500, 12500, 1250, 1000, 12500, 1250, 12500, 1000, 12500, 1250, 1250, 1250, 1250, 1000, 1250, 1000])], axis=1)
        tbl_0 = 0.05 * jax.random.normal(jax.random.fold_in(_tk, 500 + 0), (1000, 128), jnp.float32)
        tbl_1 = 0.05 * jax.random.normal(jax.random.fold_in(_tk, 500 + 1), (1250, 128), jnp.float32)
        tbl_2 = 0.05 * jax.random.normal(jax.random.fold_in(_tk, 500 + 2), (12500, 128), jnp.float32)
        tbl_3 = 0.05 * jax.random.normal(jax.random.fold_in(_tk, 500 + 3), (125000, 128), jnp.float32)
        tbl_4 = 0.05 * jax.random.normal(jax.random.fold_in(_tk, 500 + 4), (1000, 128), jnp.float32)
        tbl_5 = 0.05 * jax.random.normal(jax.random.fold_in(_tk, 500 + 5), (1000, 128), jnp.float32)
        tbl_6 = 0.05 * jax.random.normal(jax.random.fold_in(_tk, 500 + 6), (12500, 128), jnp.float32)
        tbl_7 = 0.05 * jax.random.normal(jax.random.fold_in(_tk, 500 + 7), (1250, 128), jnp.float32)
        tbl_8 = 0.05 * jax.random.normal(jax.random.fold_in(_tk, 500 + 8), (1000, 128), jnp.float32)
        tbl_9 = 0.05 * jax.random.normal(jax.random.fold_in(_tk, 500 + 9), (12500, 128), jnp.float32)
        tbl_10 = 0.05 * jax.random.normal(jax.random.fold_in(_tk, 500 + 10), (12500, 128), jnp.float32)
        tbl_11 = 0.05 * jax.random.normal(jax.random.fold_in(_tk, 500 + 11), (12500, 128), jnp.float32)
        tbl_12 = 0.05 * jax.random.normal(jax.random.fold_in(_tk, 500 + 12), (1250, 128), jnp.float32)
        tbl_13 = 0.05 * jax.random.normal(jax.random.fold_in(_tk, 500 + 13), (1000, 128), jnp.float32)
        tbl_14 = 0.05 * jax.random.normal(jax.random.fold_in(_tk, 500 + 14), (12500, 128), jnp.float32)
        tbl_15 = 0.05 * jax.random.normal(jax.random.fold_in(_tk, 500 + 15), (1250, 128), jnp.float32)
        tbl_16 = 0.05 * jax.random.normal(jax.random.fold_in(_tk, 500 + 16), (12500, 128), jnp.float32)
        tbl_17 = 0.05 * jax.random.normal(jax.random.fold_in(_tk, 500 + 17), (1000, 128), jnp.float32)
        tbl_18 = 0.05 * jax.random.normal(jax.random.fold_in(_tk, 500 + 18), (12500, 128), jnp.float32)
        tbl_19 = 0.05 * jax.random.normal(jax.random.fold_in(_tk, 500 + 19), (1250, 128), jnp.float32)
        tbl_20 = 0.05 * jax.random.normal(jax.random.fold_in(_tk, 500 + 20), (1250, 128), jnp.float32)
        tbl_21 = 0.05 * jax.random.normal(jax.random.fold_in(_tk, 500 + 21), (1250, 128), jnp.float32)
        tbl_22 = 0.05 * jax.random.normal(jax.random.fold_in(_tk, 500 + 22), (1250, 128), jnp.float32)
        tbl_23 = 0.05 * jax.random.normal(jax.random.fold_in(_tk, 500 + 23), (1000, 128), jnp.float32)
        tbl_24 = 0.05 * jax.random.normal(jax.random.fold_in(_tk, 500 + 24), (1250, 128), jnp.float32)
        tbl_25 = 0.05 * jax.random.normal(jax.random.fold_in(_tk, 500 + 25), (1000, 128), jnp.float32)
        _rk = jax.random.fold_in(_tk, 7)
        r_dense_features = -0.000520686 + 1.00062 * jax.random.normal(jax.random.fold_in(_rk, 101), (2048, 128), jnp.float32)
        W_top1 = 0.0405887 * jax.random.normal(jax.random.fold_in(_tk, 801), (607, 512), jnp.float32)
        W_top2 = 0.0441942 * jax.random.normal(jax.random.fold_in(_tk, 802), (512, 256), jnp.float32)
        W_top3 = 0.0625 * jax.random.normal(jax.random.fold_in(_tk, 803), (256, 1), jnp.float32)
        b_top1 = jnp.zeros((512,), jnp.float32)
        b_top2 = jnp.zeros((256,), jnp.float32)
        return (r_dense_features, ids, tbl_0, tbl_1, tbl_2, tbl_3, tbl_4, tbl_5, tbl_6, tbl_7, tbl_8, tbl_9, tbl_10, tbl_11, tbl_12, tbl_13, tbl_14, tbl_15, tbl_16, tbl_17, tbl_18, tbl_19, tbl_20, tbl_21, tbl_22, tbl_23, tbl_24, tbl_25, W_top1, b_top1, W_top2, b_top2, W_top3)
    r_dense_features, ids, tbl_0, tbl_1, tbl_2, tbl_3, tbl_4, tbl_5, tbl_6, tbl_7, tbl_8, tbl_9, tbl_10, tbl_11, tbl_12, tbl_13, tbl_14, tbl_15, tbl_16, tbl_17, tbl_18, tbl_19, tbl_20, tbl_21, tbl_22, tbl_23, tbl_24, tbl_25, W_top1, b_top1, W_top2, b_top2, W_top3 = _rec_inputs()

    def _L0_rec_setup():
        import jax, jax.numpy as jnp
        import numpy as np
        F = 26
        N = F + 1
        _TRIU_I, _TRIU_J = np.triu_indices(N, k=1)
        key = jax.random.key(seed)
        k1, k2 = jax.random.split(key)
        B, D = (2048, 128)
        dense_features = jax.random.normal(k1, (B, D), dtype=jnp.float32)
        sparse_features = jax.random.normal(k2, (B, F, D), dtype=jnp.float32)
        return {'dense_features': dense_features, 'sparse_features': sparse_features}
    _L0_rec_all = _L0_rec_setup()
    _L0_rec_in = {k: v for k, v in _L0_rec_all.items() if k in ()}
    del _L0_rec_all
    return {'r_dense_features': r_dense_features, 'ids': ids, 'tbl_0': tbl_0, 'tbl_1': tbl_1, 'tbl_2': tbl_2, 'tbl_3': tbl_3, 'tbl_4': tbl_4, 'tbl_5': tbl_5, 'tbl_6': tbl_6, 'tbl_7': tbl_7, 'tbl_8': tbl_8, 'tbl_9': tbl_9, 'tbl_10': tbl_10, 'tbl_11': tbl_11, 'tbl_12': tbl_12, 'tbl_13': tbl_13, 'tbl_14': tbl_14, 'tbl_15': tbl_15, 'tbl_16': tbl_16, 'tbl_17': tbl_17, 'tbl_18': tbl_18, 'tbl_19': tbl_19, 'tbl_20': tbl_20, 'tbl_21': tbl_21, 'tbl_22': tbl_22, 'tbl_23': tbl_23, 'tbl_24': tbl_24, 'tbl_25': tbl_25, 'W_top1': W_top1, 'b_top1': b_top1, 'W_top2': W_top2, 'b_top2': b_top2, 'W_top3': W_top3}

def reference(r_dense_features, ids, tbl_0, tbl_1, tbl_2, tbl_3, tbl_4, tbl_5, tbl_6, tbl_7, tbl_8, tbl_9, tbl_10, tbl_11, tbl_12, tbl_13, tbl_14, tbl_15, tbl_16, tbl_17, tbl_18, tbl_19, tbl_20, tbl_21, tbl_22, tbl_23, tbl_24, tbl_25, W_top1, b_top1, W_top2, b_top2, W_top3):
    import jax
    import jax.numpy as jnp

    def _L0_rec_ref(dense_features, sparse_features):
        import jax, jax.numpy as jnp
        import numpy as np
        F = 26
        N = F + 1
        _TRIU_I, _TRIU_J = np.triu_indices(N, k=1)
        combined = jnp.concatenate([dense_features[:, None, :], sparse_features], axis=1)
        interactions = jnp.einsum('bnd,bmd->bnm', combined, combined)
        interactions_flat = interactions[:, _TRIU_I, _TRIU_J]
        return jnp.concatenate([dense_features, interactions_flat], axis=1)
    e = jnp.stack([tbl_0[ids[:, 0]], tbl_1[ids[:, 1]], tbl_2[ids[:, 2]], tbl_3[ids[:, 3]], tbl_4[ids[:, 4]], tbl_5[ids[:, 5]], tbl_6[ids[:, 6]], tbl_7[ids[:, 7]], tbl_8[ids[:, 8]], tbl_9[ids[:, 9]], tbl_10[ids[:, 10]], tbl_11[ids[:, 11]], tbl_12[ids[:, 12]], tbl_13[ids[:, 13]], tbl_14[ids[:, 14]], tbl_15[ids[:, 15]], tbl_16[ids[:, 16]], tbl_17[ids[:, 17]], tbl_18[ids[:, 18]], tbl_19[ids[:, 19]], tbl_20[ids[:, 20]], tbl_21[ids[:, 21]], tbl_22[ids[:, 22]], tbl_23[ids[:, 23]], tbl_24[ids[:, 24]], tbl_25[ids[:, 25]]], axis=1)
    z = _L0_rec_ref(r_dense_features, e)
    z = z.reshape(z.shape[0], -1)
    h = jnp.concatenate([z, r_dense_features], axis=1)
    h = jnp.maximum(h @ W_top1 + b_top1, 0.0)
    h = jnp.maximum(h @ W_top2 + b_top2, 0.0)
    y = h @ W_top3
    return y

_drawn_inputs = setup_inputs


def setup_inputs(seed=0):
    import zlib

    import numpy as np

    out = dict(_drawn_inputs(seed))
    spreads = {'b_top1': (0.0, 0.1), 'b_top2': (0.0, 0.1)}
    factors = {}
    for name, (base, spread) in spreads.items():
        noise = np.random.default_rng([zlib.crc32(name.encode()), seed]).standard_normal(out[name].shape)
        drawn = base * np.exp(spread * noise) if base else spread * noise
        out[name] = jnp.asarray(drawn.astype(out[name].dtype))
    for name, factor in factors.items():
        out[name] = (out[name] * factor).astype(out[name].dtype)
    return out
```

```python
from contextlib import ExitStack

import concourse.bass as bass
from concourse import mybir

P = 128
ALU = mybir.AluOpType
ACT = mybir.ActivationFunctionType
F32 = mybir.dt.float32
I32 = mybir.dt.int32
U32 = mybir.dt.uint32


def dlrm_tower(nc, dense, ids, tables, w1, b1, w2, b2, w3, out):
    B, D = dense.shape
    F = len(tables)
    N = F + 1
    H1, H2 = w1.shape[1], w2.shape[1]
    M1, M2 = H1 // P, H2 // P
    PAIRS = N * (N - 1) // 2
    assert D == P and B % (2 * P) == 0 and w1.shape[0] == 2 * D + PAIRS
    ROUNDS = B // (2 * P)

    Q = 4
    QS = P // Q
    J = N - 1
    JG = -(-J // Q)
    jcount = [min(JG, J - g * JG) for g in range(Q)]
    HALF = QS // 2

    TG = 4
    groups = [list(range(f, min(f + TG, N))) for f in range(0, N, TG)]
    NG = len(groups)

    def pair_row(i, j):
        return D + i * N - i * (i + 1) // 2 + (j - i - 1)

    with ExitStack() as ctx:
        def sb(name, shape, dt=F32):
            return ctx.enter_context(nc.sbuf_tensor(name, shape, dt))

        def ps(name, shape):
            return ctx.enter_context(nc.psum_tensor(name, shape, F32))

        def sem(name):
            return ctx.enter_context(nc.semaphore(name))

        ident = sb("ident", [P, P])
        ones = sb("ones", [P, P])
        idx = [sb(f"idx{u}", [P, F], I32) for u in range(2)]
        rows = [sb(f"rows{u}", [P, N, D]) for u in range(2)]
        vecs = sb("vecs", [P, P, N])
        inter = sb("inter", [P, JG, P])
        w_pair = sb("w_pair", [P, JG, H1])
        w_dense = sb("w_dense", [P, H1])
        w_dense2 = sb("w_dense2", [P, H1])
        w2_sb = sb("w2_sb", [P, M1, H2])
        w3_sb = sb("w3_sb", [P, M2])
        b1_sb = sb("b1_sb", [P, M1])
        b2_sb = sb("b2_sb", [P, M2])
        h1_sb = sb("h1_sb", [P, M1, P])
        h2_sb = sb("h2_sb", [P, M2, P])
        y_sb = sb("y_sb", [P, B // P])
        y_rows = sb("y_rows", [B // P, P])

        vec_ps = [ps(f"vec_ps{k}", [P, 512]) for k in range(2)]
        dots_ps = ps("dots_ps", [P, 2, 512])
        h1_ps = [ps(f"h1_ps{h}", [P, M1 // 2, 256]) for h in range(2)]
        h2_ps = ps("h2_ps", [P, M2, 256])
        y_ps = ps("y_ps", [P, 512])

        ones_set = sem("ones_set")
        ident_made = sem("ident_made")
        pads_zero = sem("pads_zero")
        pair_w_in = sem("pair_w_in")
        dense_w_in = sem("dense_w_in")
        mlp_w_in = sem("mlp_w_in")
        dense_w_sum = sem("dense_w_sum")
        idx_in = [sem(f"idx_in{u}") for u in range(2)]
        dense_in = [sem(f"dense_in{u}") for u in range(2)]
        gathered = [[sem(f"gathered{u}_{k}") for k in range(NG)] for u in range(2)]
        tiles_begun = sem("tiles_begun")
        transposed = sem("transposed")
        vecs_by_act = sem("vecs_by_act")
        vecs_by_dve = sem("vecs_by_dve")
        dots_done = sem("dots_done")
        inter_by_act = sem("inter_by_act")
        inter_by_dve = sem("inter_by_dve")
        h1_done = sem("h1_done")
        relu1_by_act = sem("relu1_by_act")
        relu1_by_dve = sem("relu1_by_dve")
        h2_done = sem("h2_done")
        relu2_by_act = sem("relu2_by_act")
        y_done = sem("y_done")
        y_kept = sem("y_kept")
        y_turned = sem("y_turned")
        y_ready = sem("y_ready")
        out_written = sem("out_written")

        n_pair_dmas = sum(1 for i in range(N - 1) for g in range(Q)
                          if max(i + 1, g * JG + 1) <= g * JG + jcount[g])

        block = ctx.enter_context(nc.Block())

        @block.sync
        def _(sp):
            def load_tile(i, u):
                t0 = i * (2 * P) + u * P
                sp.dma_start(idx[u][:], ids[bass.ds(t0, P), :]).then_inc(idx_in[u], 16)
                sp.dma_start(rows[u][:, 0, :], dense[bass.ds(t0, P), :]).then_inc(dense_in[u], 16)

            for u in range(2):
                load_tile(0, u)
            with nc.allow_non_contiguous_dma(reason="a few hundred numbers, once"):
                sp.dma_start(b1_sb[:], b1.rearrange("(m p) -> p m", p=P)).then_inc(mlp_w_in, 16)
                sp.dma_start(b2_sb[:], b2.rearrange("(m p) -> p m", p=P)).then_inc(mlp_w_in, 16)
                sp.dma_start(w3_sb[:], w3.rearrange("(m p) o -> p (m o)", p=P)).then_inc(mlp_w_in, 16)
            sp.dma_start(w_dense[:], w1[0:D, :]).then_inc(dense_w_in, 16)
            sp.dma_start(w_dense2[:], w1[D + PAIRS:2 * D + PAIRS, :]).then_inc(dense_w_in, 16)
            sp.dma_start(w2_sb[:], w2.rearrange("(m p) n -> p m n", p=P)).then_inc(mlp_w_in, 16)
            sp.wait_ge(pads_zero, 1)
            for i in range(N - 1):
                for g in range(Q):
                    j0, j1 = max(i + 1, g * JG + 1), g * JG + jcount[g]
                    if j0 <= j1:
                        p, r = g * QS + i, pair_row(i, j0)
                        sp.dma_start(w_pair[p:p + 1, j0 - 1 - g * JG:j1 - g * JG, :],
                                     w1[r:r + j1 - j0 + 1, :].rearrange("(a r) n -> a r n", a=1)
                                     ).then_inc(pair_w_in, 16)
            with sp.Fori(0, ROUNDS - 1) as i:
                for u in range(2):
                    sp.wait_ge(transposed, i * (2 * NG) + (u + 1) * NG)
                    load_tile(i + 1, u)
            sp.wait_ge(y_ready, 1)
            sp.dma_start(out.rearrange("(t p) o -> t (p o)", p=P), y_rows[:]).then_inc(out_written, 16)
            sp.wait_ge(out_written, 16)

        @block.gpsimd
        def _(pool):
            def gather_tile(u):
                for k, group in enumerate(groups):
                    for f in group:
                        if f:
                            nc.gpsimd.indirect_dma_start(
                                out=rows[u][:, f, :], out_offset=None, in_=tables[f - 1][:, :],
                                in_offset=bass.IndirectOffsetOnAxis(ap=idx[u][:, f - 1:f].bitcast(U32), axis=0),
                            ).then_inc(gathered[u][k], 16)

            pool.memset(ones[:], 1.0).then_inc(ones_set, 1)
            pool.wait_ge(ones_set, 1)
            pool.affine_select(out=ident[:], in_=ones[:], compare_op=ALU.is_equal, fill=0.0, base=0,
                               pattern=[[-1, P]], channel_multiplier=1).then_inc(ident_made, 1)
            with pool.Fori(0, ROUNDS) as i:
                for u in range(2):
                    pool.wait_ge(idx_in[u], i * 16 + 16)
                    pool.sem_inc(tiles_begun, 1)
                    gather_tile(u)

        @block.tensor
        def _(pe):
            pe.wait_ge(ident_made, 1)

            def one_tile(i, u):
                for k, group in enumerate(groups):
                    kk = u * NG + k
                    n_gathers = len([f for f in group if f])
                    pe.wait_ge(gathered[u][k], i * (16 * n_gathers) + 16 * n_gathers)
                    if k == 0:
                        pe.wait_ge(dense_in[u], i * 16 + 16)
                    freed = vecs_by_dve if kk % 2 else vecs_by_act
                    pe.wait_ge(freed, i * NG + kk // 2 + 1)
                    for s, f in enumerate(group):
                        last = pe.transpose(vec_ps[kk % 2][:, s * P:(s + 1) * P], rows[u][:, f, :], ident[:])
                    last.then_inc(transposed, 1)

            def dots(i, u):
                end = (u + 1) * NG
                pe.wait_ge(vecs_by_act, i * NG + (end + 1) // 2 + 1)
                pe.wait_ge(vecs_by_dve, i * NG + end // 2 + 1)
                for b in range(P):
                    q, n = b // QS, b % QS
                    o = (n % HALF) * J
                    last = pe.matmul(dots_ps[q * 32:q * 32 + N, n // HALF, o:o + J], vecs[:, b, :],
                                     vecs[:, b, 1:N], start=True, stop=True)
                last.then_inc(dots_done, 1)

            def mlp(i, u):
                if u == 0:
                    pe.wait_ge(pair_w_in, 16 * n_pair_dmas)
                    pe.wait_ge(dense_w_sum, 1)
                    pe.wait_ge(mlp_w_in, 64)
                pe.wait_ge(inter_by_act, i * 16 + (u + 1) * 8)
                pe.wait_ge(inter_by_dve, i * 16 + (u + 1) * 8)
                for m in range(M1):
                    c = slice(m * P, (m + 1) * P)
                    pe.matmul(h1_ps[m * 2 // M1][:, m % 2, 0:P], w_dense[:, c], vecs[:, :, 0], start=True, stop=False)
                    for jj in range(JG):
                        last = pe.matmul(h1_ps[m * 2 // M1][:, m % 2, 0:P], w_pair[:, jj, c], inter[:, jj, :],
                                         start=False, stop=(jj == JG - 1))
                    if m % 2:
                        last.then_inc(h1_done, 1)
                pe.wait_ge(relu1_by_act, i * 4 + (u + 1) * 2)
                pe.wait_ge(relu1_by_dve, i * 4 + (u + 1) * 2)
                for m in range(M2):
                    for k in range(M1):
                        last = pe.matmul(h2_ps[:, m, 0:P], w2_sb[:, k, m * P:(m + 1) * P], h1_sb[:, k, :],
                                         start=(k == 0), stop=(k == M1 - 1))
                last.then_inc(h2_done, 1)
                pe.wait_ge(relu2_by_act, i * 4 + u * 2 + 2)
                for k in range(M2):
                    last = pe.matmul(y_ps[:, 0:1], h2_sb[:, k, :], w3_sb[:, k:k + 1],
                                     start=(k == 0), stop=(k == M2 - 1))
                last.then_inc(y_done, 1)

            def round_(i):
                for u in range(2):
                    one_tile(i, u)
                    dots(i, u)
                    mlp(i, u)

            with pe.Fori(0, ROUNDS) as i:
                round_(i)
            pe.wait_ge(y_kept, B // P)
            pe.transpose(h2_ps[0:B // P, 0, 0:P], y_sb[:], ident[:]).then_inc(y_turned, 1)

        def copy_vecs(eng, copy, i, u, k, done):
            kk = u * NG + k
            group = groups[k]
            eng.wait_ge(transposed, i * (2 * NG) + kk + 1)
            n = len(group)
            copy(vecs[:, :, group[0]:group[0] + n].rearrange("p b f -> p f b"),
                 vec_ps[kk % 2][:, 0:n * P].rearrange("p (f b) -> p f b", f=n)).then_inc(done, 1)

        def copy_inter(copy, q, g, done):
            n = jcount[g]
            src = dots_ps[q * 32:q * 32 + N, :, 0:HALF * J].rearrange(
                "p h (s j) -> p j h s", j=J)[:, g * JG:g * JG + n]
            dst = inter[g * 32:g * 32 + N, 0:n, q * QS:(q + 1) * QS].rearrange("p j (h s) -> p j h s", h=2)
            copy(dst, src).then_inc(done, 1)

        @block.scalar
        def _(act):
            act.sem_inc(vecs_by_act, 1)
            act.wait_ge(mlp_w_in, 64)
            act.wait_ge(pads_zero, 2)
            with act.Fori(0, ROUNDS) as i:
                for u in range(2):
                    for k in range(NG):
                        if (u * NG + k) % 2 == 0:
                            copy_vecs(act, nc.scalar.copy, i, u, k, vecs_by_act)
                    act.wait_ge(dots_done, i * 2 + u + 1)
                    for q in range(0, 2):
                        for g in range(Q):
                            copy_inter(nc.scalar.copy, q, g, inter_by_act)
                    act.wait_ge(h1_done, i * 4 + u * 2 + 1)
                    for m in range(M1 // 2):
                        nc.scalar.activation(h1_sb[:, m, :], h1_ps[0][:, m, 0:P], ACT.Relu,
                                             bias=b1_sb[:, m:m + 1]).then_inc(relu1_by_act, 1)
                    act.wait_ge(h2_done, i * 2 + u + 1)
                    for m in range(M2):
                        nc.scalar.activation(h2_sb[:, m, :], h2_ps[:, m, 0:P], ACT.Relu,
                                             bias=b2_sb[:, m:m + 1]).then_inc(relu2_by_act, 1)

        @block.vector
        def _(dve):
            dve.sem_inc(vecs_by_dve, 1)
            dve.memset(w_pair[:], 0.0).then_inc(pads_zero, 1)
            dve.memset(inter[:], 0.0).then_inc(pads_zero, 1)
            dve.wait_ge(dense_w_in, 32)
            dve.tensor_tensor(w_dense[:], w_dense[:], w_dense2[:], ALU.add).then_inc(dense_w_sum, 1)
            dve.wait_ge(mlp_w_in, 64)
            dve.wait_ge(pads_zero, 2)
            with dve.Fori(0, ROUNDS) as i:
                for u in range(2):
                    for k in range(NG):
                        if (u * NG + k) % 2 == 1:
                            copy_vecs(dve, dve.tensor_copy, i, u, k, vecs_by_dve)
                    dve.wait_ge(dots_done, i * 2 + u + 1)
                    for q in range(2, 4):
                        for g in range(Q):
                            copy_inter(dve.tensor_copy, q, g, inter_by_dve)
                    dve.wait_ge(h1_done, i * 4 + u * 2 + 2)
                    for m in range(M1 // 2, M1):
                        dve.tensor_scalar(h1_sb[:, m, :], h1_ps[1][:, m % 2, 0:P], b1_sb[:, m:m + 1], 0.0,
                                          ALU.add, ALU.max).then_inc(relu1_by_dve, 1)
                    dve.wait_ge(y_done, i * 2 + u + 1)
                    dve.tensor_copy(y_sb[:, bass.ds(i * 2 + u, 1)], y_ps[:, 0:1]).then_inc(y_kept, 1)
            dve.wait_ge(y_turned, 1)
            dve.tensor_copy(y_rows[:], h2_ps[0:B // P, 0, 0:P]).then_inc(y_ready, 1)


TABLES = [f"tbl_{f}" for f in range(26)]
INPUTS = ["r_dense_features", "ids", *TABLES, "W_top1", "b_top1", "W_top2", "b_top2", "W_top3"]


def kernel(**inputs):
    import numpy as np
    import concourse.bacc as bacc
    from concourse.bass_utils import run_bass_kernel_spmd

    nc = bacc.Bacc("TRN2", target_bir_lowering=False, num_devices=1)
    arrays, aps = {}, {}
    for name in INPUTS:
        a = np.ascontiguousarray(inputs[name])
        arrays[f"in_{name}"] = a
        aps[name] = nc.dram_tensor(f"in_{name}", a.shape, mybir.dt.from_np(a.dtype), kind="ExternalInput").ap()
    batch = aps["r_dense_features"].shape[0]
    out = nc.dram_tensor("out", (batch, 1), F32, kind="ExternalOutput").ap()
    dlrm_tower(nc, aps["r_dense_features"], aps["ids"], [aps[t] for t in TABLES],
               aps["W_top1"], aps["b_top1"], aps["W_top2"], aps["b_top2"], aps["W_top3"], out)
    r = run_bass_kernel_spmd(nc, [arrays], core_ids=[0])
    return r.results[0]["out"]
```

```python
from contextlib import ExitStack

import concourse.bass as bass
from concourse import mybir

P = 128
ALU = mybir.AluOpType
ACT = mybir.ActivationFunctionType
F32 = mybir.dt.float32
I32 = mybir.dt.int32
F16 = mybir.dt.float16
U32 = mybir.dt.uint32
F32R = mybir.dt.float32r
SPREAD = (5, 6, 9, 24, 26)


def dlrm_tower(nc, dense, ids, tables, w1, w1_laid, b1, w2, b2, w3, out):
    B, D = dense.shape
    F = len(tables)
    N = F + 1
    H1, H2 = w1.shape[1], w2.shape[1]
    M1, M2 = H1 // P, H2 // P
    L2 = M1 * M2
    PAIRS = N * (N - 1) // 2
    R = 2 * P
    ROUNDS = B // R
    assert D == P and B % (2 * R) == 0 and w1.shape[0] == 2 * D + PAIRS
    PASSES = ROUNDS // 2

    Q = 4
    QS = P // Q
    J = N - 1
    JG = -(-J // Q)
    jcount = [min(JG, J - g * JG) for g in range(Q)]
    HALF = QS // 2
    ACT_Q = 3
    NA, ND = ACT_Q * Q + 1, (Q - ACT_Q) * Q

    rest = [f for f in range(N) if f not in SPREAD]
    groups = []
    for f in rest:
        g = groups[-1] if groups else None
        if g and len(g) < 4 and (len(g) == 1 or f - g[-1] == g[1] - g[0]):
            g.append(f)
        else:
            groups.append([f])
    NG = len(groups)
    X = len(SPREAD)
    V = tables[SPREAD[0] - 1].shape[0]
    KT = 8
    KP = V // KT
    assert V == KP * KT and KP <= P and all(tables[f - 1].shape[0] == V for f in SPREAD)
    KH = KT // 2
    PLACES = 6
    EARLY = 3
    assert X <= PLACES
    at_place = {k: k for k in range(X)}

    with ExitStack() as ctx:
        def sb(name, shape, dt=F32):
            return ctx.enter_context(nc.sbuf_tensor(name, shape, dt))

        def ps(name, shape):
            return ctx.enter_context(nc.psum_tensor(name, shape, F32))

        def sem(name):
            return ctx.enter_context(nc.semaphore(name))

        ident = sb("ident", [P, P])
        ones = sb("ones", [P, P])
        idx = [sb(f"idx{v}", [P, F], I32) for v in range(4)]
        rows = [sb(f"rows{u}", [P, len(rest), D]) for u in range(2)]
        vecs = [sb(f"vecs{s}", [P, 2, P, N]) for s in range(2)]
        inter = sb("inter", [P, JG + 1, P])
        x_hi = sb("x_hi", [P, JG + 1, R], F32R)
        x_lo = sb("x_lo", [P, JG + 1, R], F32R)
        w_hi = sb("w_hi", [P, JG + 1, H1], F32R)
        w_lo = sb("w_lo", [P, JG + 1, H1], F32R)
        w2_sb = sb("w2_sb", [P, M1, H2])
        w3_sb = sb("w3_sb", [P, M2])
        b1_sb = sb("b1_sb", [P, M1])
        b2_sb = sb("b2_sb", [P, M2])
        h1_sb = sb("h1_sb", [P, M1, R])
        h2_sb = sb("h2_sb", [P, M2, R])
        y_sb = sb("y_sb", [P, B // P])
        y_rows = sb("y_rows", [B // P, P])
        ids_all = h1_sb[:, 0:2, :].rearrange("p m r -> p (m r)")[:, 0:B // P * F].bitcast(I32).rearrange(
            "p (t f) -> p t f", f=F)
        w_dense2 = sb("w_dense2", [P, H1])
        ids_f = w_dense2[:, 0:B // P * X].rearrange("p (t k) -> p t k", k=X)
        ids_t = sb("ids_t", [X, B], F16)
        pick_f = inter[0:X, 0:X, :]
        pick = sb("pick", [X, X, P], F16)
        row_of_i = sb("row_of_i", [P, KT], I32)
        row_of = sb("row_of", [P, KT])
        stage = [sb(f"stage{s}", [P, KT * D]) for s in range(2)]
        WP = KT * D // H1
        N_PIECES = X + (JG + 1) // WP
        assert KT * D % H1 == 0 and (JG + 1) % WP == 0
        t_hi = sb("t_hi", [P, X, KT, D], F32R)
        t_lo = sb("t_lo", [P, X, KT, D], F32R)

        def piece(n, hi):
            if n < X:
                return (t_hi if hi else t_lo)[0:KP, n].rearrange("p t d -> p (t d)")
            a = (n - X) * WP
            return (w_hi if hi else w_lo)[:, a:a + WP, :].rearrange("p j n -> p (j n)")

        def staged_piece(n):
            return stage[n % 2][0:KP] if n < X else stage[n % 2][:]

        onehot = [sb(f"onehot{h}", [P, KH, R], F32R) for h in range(2)]

        vec_ps = [ps(f"vec_ps{k}", [P, 512]) for k in range(2)]
        dots_ps = ps("dots_ps", [P, 2, 512])
        h1_ps = ps("h1_ps", [P, M1 // 2, R])
        h2_ps = ps("h2_ps", [P, M2, R])
        ids_ps = ps("ids_ps", [P, 512])
        fetch_ps = ps("fetch_ps", [P, 512])

        ones_set = sem("ones_set")
        ident_made = sem("ident_made")
        picks_zero = sem("picks_zero")
        picks_made = sem("picks_made")
        picks_cast = sem("picks_cast")
        rows_counted = sem("rows_counted")
        rows_cast = sem("rows_cast")
        ids_in = sem("ids_in")
        ids_cast = sem("ids_cast")
        ids_turned = sem("ids_turned")
        ids_ready = sem("ids_ready")
        staged = [sem(f"staged{s}") for s in range(2)]
        hi_made = sem("hi_made")
        lo_made = sem("lo_made")
        pads_zero = sem("pads_zero")
        dense_w_in = sem("dense_w_in")
        mlp_w_in = sem("mlp_w_in")
        dense_w_sum = sem("dense_w_sum")
        x_hi_made = sem("x_hi_made")
        x_lo_made = sem("x_lo_made")
        idx_in = [sem(f"idx_in{v}") for v in range(4)]
        dense_in = [sem(f"dense_in{u}") for u in range(2)]
        gathered = [[sem(f"gathered{u}_{k}") for k in range(NG)] for u in range(2)]
        tiles_begun = sem("tiles_begun")
        transposed = sem("transposed")
        vecs_by_act = sem("vecs_by_act")
        vecs_by_dve = sem("vecs_by_dve")
        ids_spread = sem("ids_spread")
        compared = sem("compared")
        onehot_used = sem("onehot_used")
        fetched = sem("fetched")
        dots_done = sem("dots_done")
        inter_by_act = sem("inter_by_act")
        inter_by_dve = sem("inter_by_dve")
        h1_done = sem("h1_done")
        relu1_done = sem("relu1_done")
        h2_done = sem("h2_done")
        relu2_done = sem("relu2_done")
        y_done = sem("y_done")
        y_kept = sem("y_kept")
        y_turned = sem("y_turned")
        y_ready = sem("y_ready")
        out_written = sem("out_written")

        def groups_of(tiles):
            return (tiles + 2) * NG

        def items(i, r):
            if isinstance(i, int) and 2 * i + r + 1 == ROUNDS:
                return {}
            return {place: (k, i * (2 * X) + (r + 1) * X + k) for place, k in at_place.items()}

        def passes(eng, step):
            step((0, 0), None)
            with eng.Fori(0, PASSES - 1) as i:
                step((i, 1), (i, 0))
                step((i + 1, 0), (i, 1))
            step((PASSES - 1, 1), (PASSES - 1, 0))
            step(None, (PASSES - 1, 1))

        block = ctx.enter_context(nc.Block())

        @block.sync
        def _(sp):
            def load_idx(i, v):
                sp.dma_start(idx[v][:], ids[bass.ds(i * (4 * P) + v * P, P), :]).then_inc(idx_in[v], 16)

            def load_dense(i, v):
                u = v % 2
                sp.dma_start(rows[u][:, 0, :], dense[bass.ds(i * (4 * P) + v * P, P), :]).then_inc(dense_in[u], 16)

            load_idx(0, 0)
            sp.dma_start(ids_all, ids.rearrange("(t p) f -> p t f", p=P)).then_inc(ids_in, 16)
            for v in range(1, 4):
                load_idx(0, v)
            for v in range(2):
                load_dense(0, v)
            for n in range(N_PIECES):
                if n == X:
                    sp.wait_ge(ids_turned, 4)
                    sp.dma_start(w_dense2[:], w1[D + PAIRS:2 * D + PAIRS, :]).then_inc(dense_w_in, 16)
                if n >= 2:
                    sp.wait_ge(hi_made, n - 1)
                    sp.wait_ge(lo_made, n - 1)
                if n < X:
                    src = tables[SPREAD[n] - 1].rearrange("(p t) d -> p (t d)", t=KT)
                else:
                    src = w1_laid[:, (n - X) * WP * H1:(n - X + 1) * WP * H1]
                sp.dma_start(staged_piece(n), src).then_inc(staged[n % 2], 16)
                if n == 1:
                    with nc.allow_non_contiguous_dma(reason="a few hundred numbers, once"):
                        sp.dma_start(b1_sb[:], b1.rearrange("(m p) -> p m", p=P)).then_inc(mlp_w_in, 16)
                        sp.dma_start(b2_sb[:], b2.rearrange("(m p) -> p m", p=P)).then_inc(mlp_w_in, 16)
                        sp.dma_start(w3_sb[:], w3.rearrange("(m p) o -> p (m o)", p=P)).then_inc(mlp_w_in, 16)
                    sp.dma_start(w2_sb[:], w2.rearrange("(m p) n -> p m n", p=P)).then_inc(mlp_w_in, 16)

            def refill(i, v, more):
                sp.wait_ge(transposed, i * (4 * NG) + groups_of(v + 1))
                load_dense(*((i, v + 2) if v < 2 else (i + 1, v - 2)))
                if more:
                    load_idx(i + 1, v)

            with sp.Fori(0, PASSES - 1) as i:
                for v in range(4):
                    refill(i, v, True)
            for v in range(2):
                refill(PASSES - 1, v, False)
            sp.wait_ge(y_ready, 1)
            sp.dma_start(out.rearrange("(t p) o -> t (p o)", p=P), y_rows[:]).then_inc(out_written, 16)
            sp.wait_ge(out_written, 16)

        @block.gpsimd
        def _(pool):
            def gather_tile(v):
                for k, group in enumerate(groups):
                    for f in group:
                        if f:
                            nc.gpsimd.indirect_dma_start(
                                out=rows[v % 2][:, rest.index(f), :], out_offset=None, in_=tables[f - 1][:, :],
                                in_offset=bass.IndirectOffsetOnAxis(ap=idx[v][:, f - 1:f].bitcast(U32), axis=0),
                            ).then_inc(gathered[v % 2][k], 16)

            pool.iota(row_of_i[:], pattern=[[1, KT]], base=0, channel_multiplier=KT).then_inc(rows_counted, 1)
            pool.memset(ones[:], 1.0).then_inc(ones_set, 1)
            pool.memset(pick_f, 0.0).then_inc(picks_zero, 1)
            pool.wait_ge(ones_set, 1)
            pool.affine_select(out=ident[:], in_=ones[:], compare_op=ALU.is_equal, fill=0.0, base=0,
                               pattern=[[-1, P]], channel_multiplier=1).then_inc(ident_made, 1)
            pool.wait_ge(picks_zero, 1)
            pool.affine_select(out=pick_f, in_=pick_f, compare_op=ALU.not_equal, fill=1.0, base=0,
                               pattern=[[-1, X], [0, P]], channel_multiplier=1).then_inc(picks_made, 1)
            with pool.Fori(0, PASSES) as i:
                for v in range(4):
                    pool.wait_ge(idx_in[v], i * 16 + 16)
                    pool.wait_ge(transposed, i * (4 * NG) + groups_of(v - 1))
                    pool.sem_inc(tiles_begun, 1)
                    gather_tile(v)

        @block.tensor
        def _(pe):
            def transpose_rows(i, v, layer2_of=None):
                u = v % 2
                for k, group in enumerate(groups):
                    kk = v * NG + k
                    n_gathers = len([f for f in group if f])
                    pe.wait_ge(gathered[u][k], i * (32 * n_gathers) + (v // 2 + 1) * 16 * n_gathers)
                    if k == 0:
                        pe.wait_ge(dense_in[u], i * 32 + (v // 2 + 1) * 16)
                    freed = vecs_by_dve if kk % 2 else vecs_by_act
                    pe.wait_ge(freed, i * (2 * NG) + kk // 2 + 1)
                    for s, f in enumerate(group):
                        last = pe.transpose(vec_ps[kk % 2][:, s * P:(s + 1) * P], rows[u][:, rest.index(f), :],
                                            ident[:])
                    last.then_inc(transposed, 1)
                    if layer2_of:
                        layer2(*layer2_of, range(k * L2 // NG, (k + 1) * L2 // NG))

            def dots(i, v):
                end = (v + 1) * NG
                vs = vecs[v // 2][:, v % 2]
                pe.wait_ge(vecs_by_act, i * (2 * NG) + (end + 1) // 2 + 1)
                pe.wait_ge(vecs_by_dve, i * (2 * NG) + end // 2 + 1)
                if v % 2 == 0:
                    pe.wait_ge(fetched, i * (2 * X) + (v // 2 + 1) * X)
                for b in range(P):
                    q, n = b // QS, b % QS
                    o = (n % HALF) * J
                    last = pe.matmul(dots_ps[q * 32:q * 32 + N, n // HALF, o:o + J], vs[:, b, :],
                                     vs[:, b, 1:N], start=True, stop=True)
                last.then_inc(dots_done, 1)

            def spread_ids(round_, k):
                pe.matmul(ids_ps[:, 0:R], pick[:, k, :], ids_t[:, bass.ds(round_ * R, R)],
                          start=True, stop=True).then_inc(ids_spread, 1)

            def fetch(k, m, for_round):
                pe.wait_ge(compared, m * 2 + 2)
                if not (isinstance(m, int) and m == 0):
                    pe.wait_ge(fetched, m)
                for h in range(2):
                    for t in range(KH):
                        for part in (t_hi, t_lo):
                            last = pe.matmul(fetch_ps[:, 0:R], part[0:KP, k, h * KH + t, :], onehot[h][0:KP, t, :],
                                             start=(h == 0 and t == 0 and part is t_hi),
                                             stop=(h == 1 and t == KH - 1 and part is t_lo))
                    last.then_inc(onehot_used, 1)
                    if h == 0 and k < X - 1:
                        spread_ids(for_round, k + 1)

            def place(i, v, n):
                work = items(i, v // 2)
                if (v % 2) * 3 + n in work:
                    k, m = work[(v % 2) * 3 + n]
                    fetch(k, m, i * 2 + v // 2 + 1)

            def layer1(i, r, half):
                if half == 0:
                    pe.wait_ge(lo_made, N_PIECES)
                    pe.wait_ge(x_lo_made, i * 4 + (r + 1) * 2)
                    pe.wait_ge(y_kept, i * 2 + r + 1)
                else:
                    pe.wait_ge(relu1_done, i * (2 * M1) + r * M1 + M1 // 2)
                for m in range(M1 // 2):
                    c0 = (half * (M1 // 2) + m) * P
                    for jj in range(JG + 1):
                        w_h, w_l = w_hi[:, jj, c0:c0 + P], w_lo[:, jj, c0:c0 + P]
                        pe.matmul(h1_ps[:, m, :], w_h, x_hi[:, jj, :], start=(jj == 0), stop=False)
                        pe.matmul(h1_ps[:, m, :], w_h, x_lo[:, jj, :], start=False, stop=False)
                        last = pe.matmul(h1_ps[:, m, :], w_l, x_hi[:, jj, :], start=False, stop=(jj == JG))
                last.then_inc(h1_done, 1)

            def layer2(i, r, some):
                for n in some:
                    m, k = n // M1, n % M1
                    if n == 0:
                        pe.wait_ge(relu1_done, i * (2 * M1) + (r + 1) * M1)
                    last = pe.matmul(h2_ps[:, m, :], w2_sb[:, k, m * P:(m + 1) * P],
                                     h1_sb[:, k, :], start=(k == 0), stop=(k == M1 - 1))
                    if n == L2 - 1:
                        last.then_inc(h2_done, 1)

            def layer3(i, r):
                pe.wait_ge(relu2_done, i * (2 * M2) + (r + 1) * M2)
                for t in range(2):
                    for k in range(M2):
                        last = pe.matmul(h1_ps[:, 0, t:t + 1], h2_sb[:, k, t * P:(t + 1) * P], w3_sb[:, k:k + 1],
                                         start=(k == 0), stop=(k == M2 - 1))
                last.then_inc(y_done, 1)

            pe.sem_inc(transposed, groups_of(0))
            pe.wait_ge(ident_made, 1)
            pe.wait_ge(ids_cast, X)
            for n, bank in enumerate((vec_ps[0], vec_ps[1], ids_ps, fetch_ps)):
                for t in range(4):
                    last = pe.transpose(bank[0:X, t * P:(t + 1) * P], ids_f[:, 4 * n + t, :], ident[:])
                last.then_inc(ids_turned, 1)
            pe.wait_ge(ids_ready, 4)
            pe.wait_ge(picks_cast, 1)
            def fetch_first(items_):
                for k in items_:
                    pe.wait_ge(hi_made, k + 1)
                    pe.wait_ge(lo_made, k + 1)
                    fetch(k, k, 0)

            def step(now, prev):
                if now:
                    i, v = now[0], now[1] * 2
                if now and not prev:
                    spread_ids(0, 0)
                    fetch_first(range(EARLY))
                    transpose_rows(i, v)
                    fetch_first(range(EARLY, X))
                    spread_ids(1, 0)
                elif now:
                    if items(*now):
                        spread_ids(i * 2 + now[1] + 1, 0)
                    transpose_rows(i, v)
                if prev:
                    layer1(*prev, 0)
                if now:
                    place(i, v, 0)
                if prev:
                    layer1(*prev, 1)
                if now:
                    dots(i, v)
                    place(i, v, 1)
                    transpose_rows(i, v + 1, prev)
                    place(i, v, 2)
                else:
                    layer2(*prev, range(L2))
                if prev:
                    layer3(*prev)
                if now:
                    place(i, v + 1, 0)
                    dots(i, v + 1)
                    place(i, v + 1, 1)
                    place(i, v + 1, 2)

            pe.wait_ge(mlp_w_in, 64)
            passes(pe, step)
            pe.wait_ge(y_kept, ROUNDS + 1)
            pe.transpose(h2_ps[0:B // P, 0, 0:P], y_sb[:], ident[:]).then_inc(y_turned, 1)

        def copy_vecs(eng, copy, i, v, k, done):
            kk = v * NG + k
            group = groups[k]
            n = len(group)
            step = group[1] - group[0] if n > 1 else 1
            eng.wait_ge(transposed, i * (4 * NG) + groups_of(0) + kk + 1)
            copy(vecs[v // 2][:, v % 2, :, group[0]:group[-1] + 1:step].rearrange("p b f -> p f b"),
                 vec_ps[kk % 2][:, 0:n * P].rearrange("p (f b) -> p f b", f=n)).then_inc(done, 1)

        def copy_inter(copy, q, g, done):
            n = jcount[g]
            src = dots_ps[q * 32:q * 32 + N, :, 0:HALF * J].rearrange(
                "p h (s j) -> p j h s", j=J)[:, g * JG:g * JG + n]
            dst = inter[g * 32:g * 32 + N, 0:n, q * QS:(q + 1) * QS].rearrange("p j (h s) -> p j h s", h=2)
            copy(dst, src).then_inc(done, 1)

        @block.scalar
        def _(act):
            def copy_fetched(slot, k, m):
                act.wait_ge(onehot_used, m * 2 + 2)
                nc.scalar.copy(vecs[slot][:, :, :, SPREAD[k]],
                               fetch_ps[:, 0:R].rearrange("p (t b) -> p t b", t=2)).then_inc(fetched, 1)

            def place(i, v, n):
                work = items(i, v // 2)
                if (v % 2) * 3 + n in work:
                    k, m = work[(v % 2) * 3 + n]
                    copy_fetched((v // 2 + 1) % 2, k, m)

            act.sem_inc(vecs_by_act, 1)

            def split(n):
                act.wait_ge(staged[n % 2], 16 * (n // 2 + 1))
                if n == N_PIECES - 1:
                    act.wait_ge(dense_w_sum, 1)
                nc.scalar.copy(piece(n, True), staged_piece(n)).then_inc(hi_made, 1)

            for n in range(X + 2):
                if n < X:
                    split(n)
                if 2 <= n < EARLY + 2:
                    copy_fetched(0, n - 2, n - 2)

            def take_vectors(i, v):
                for k in range(NG):
                    if (v * NG + k) % 2 == 0:
                        copy_vecs(act, nc.scalar.copy, i, v, k, vecs_by_act)

            def take_products(i, v):
                act.wait_ge(dots_done, i * 4 + v + 1)
                if not (isinstance(i, int) and i == 0 and v == 0):
                    act.wait_ge(x_lo_made, i * 4 + v)
                for q in range(ACT_Q):
                    if q == 2:
                        place(i, v, 1)
                    for g in range(Q):
                        copy_inter(nc.scalar.copy, q, g, inter_by_act)
                nc.scalar.copy(inter[:, JG, :], vecs[v // 2][:, v % 2, :, 0]).then_inc(inter_by_act, 1)

            def split_input(i, v):
                act.wait_ge(inter_by_act, i * (4 * NA) + (v + 1) * NA)
                act.wait_ge(inter_by_dve, i * (4 * ND) + (v + 1) * ND)
                nc.scalar.copy(x_hi[:, :, (v % 2) * P:(v % 2 + 1) * P], inter[:]).then_inc(x_hi_made, 1)

            def rectify(i, r, what):
                if what < 2:
                    act.wait_ge(h1_done, i * 4 + r * 2 + what + 1)
                    for m in range(M1 // 2):
                        k = what * (M1 // 2) + m
                        nc.scalar.activation(h1_sb[:, k, :], h1_ps[:, m, :], ACT.Relu,
                                             bias=b1_sb[:, k:k + 1]).then_inc(relu1_done, 1)
                else:
                    act.wait_ge(h2_done, i * 2 + r + 1)
                    for m in range(M2):
                        nc.scalar.activation(h2_sb[:, m, :], h2_ps[:, m, :], ACT.Relu,
                                             bias=b2_sb[:, m:m + 1]).then_inc(relu2_done, 1)

            def step(now, prev):
                if now:
                    i, v = now[0], now[1] * 2
                    take_vectors(i, v)
                    if not prev:
                        for k in range(EARLY, X):
                            copy_fetched(0, k, k)
                if prev:
                    rectify(*prev, 0)
                if now:
                    place(i, v, 0)
                if prev:
                    rectify(*prev, 1)
                if now:
                    take_products(i, v)
                    take_vectors(i, v + 1)
                    split_input(i, v)
                if prev:
                    rectify(*prev, 2)
                if now:
                    place(i, v, 2)
                    place(i, v + 1, 0)
                    if not prev:
                        for n in range(X, N_PIECES):
                            split(n)
                    take_products(i, v + 1)
                    split_input(i, v + 1)
                    place(i, v + 1, 2)

            act.wait_ge(mlp_w_in, 64)
            act.wait_ge(pads_zero, 1)
            passes(act, step)

        @block.vector
        def _(dve):
            def compare(m):
                dve.wait_ge(ids_spread, m + 1)
                for h in range(2):
                    if not (isinstance(m, int) and m == 0):
                        dve.wait_ge(onehot_used, m * 2 - 1 + h)
                    dve.tensor_tensor(
                        onehot[h][0:KP], ids_ps[0:KP, 0:R].rearrange("p (o r) -> p o r", o=1).to_broadcast([KP, KH, R]),
                        row_of[0:KP, h * KH:(h + 1) * KH].rearrange("p (t o) -> p t o", o=1).to_broadcast([KP, KH, R]),
                        ALU.is_equal).then_inc(compared, 1)

            def place(i, v, n):
                work = items(i, v // 2)
                if (v % 2) * 3 + n in work:
                    k, m = work[(v % 2) * 3 + n]
                    if k < X - 1:
                        compare(m + 1)

            dve.sem_inc(vecs_by_dve, 1)
            dve.sem_inc(y_kept, 1)
            dve.wait_ge(ids_in, 16)
            for k, f in enumerate(SPREAD):
                dve.tensor_copy(ids_f[:, :, k], ids_all[:, :, f - 1]).then_inc(ids_cast, 1)
            dve.wait_ge(rows_counted, 1)
            dve.tensor_copy(row_of[:], row_of_i[:]).then_inc(rows_cast, 1)
            dve.wait_ge(picks_made, 1)
            dve.tensor_copy(pick[:], pick_f).then_inc(picks_cast, 1)
            for n, bank in enumerate((vec_ps[0], vec_ps[1], ids_ps, fetch_ps)):
                dve.wait_ge(ids_turned, n + 1)
                dve.tensor_copy(ids_t[:, n * 512:(n + 1) * 512], bank[0:X, :]).then_inc(ids_ready, 1)
            dve.wait_ge(rows_cast, 1)
            dve.wait_ge(picks_cast, 1)
            dve.memset(inter[:], 0.0).then_inc(pads_zero, 1)

            def split(n):
                dve.wait_ge(hi_made, n + 1)
                dve.tensor_tensor(piece(n, False), staged_piece(n), piece(n, True).bitcast(F32),
                                  ALU.subtract).then_inc(lo_made, 1)

            for k in range(X):
                split(k)
                if k < EARLY:
                    compare(k)

            def split_weights():
                for n in range(X, N_PIECES):
                    if n == N_PIECES - 1:
                        dve.wait_ge(dense_w_in, 16)
                        dve.wait_ge(staged[n % 2], 16 * (n // 2 + 1))
                        dense_part = stage[n % 2][:, (WP - 1) * H1:WP * H1]
                        dve.tensor_tensor(dense_part, dense_part, w_dense2[:], ALU.add).then_inc(dense_w_sum, 1)
                    split(n)

            def take_vectors(i, v):
                for k in range(NG):
                    if (v * NG + k) % 2 == 1:
                        copy_vecs(dve, dve.tensor_copy, i, v, k, vecs_by_dve)

            def take_products(i, v):
                dve.wait_ge(dots_done, i * 4 + v + 1)
                if not (isinstance(i, int) and i == 0 and v == 0):
                    dve.wait_ge(x_lo_made, i * 4 + v)
                for q in range(ACT_Q, Q):
                    for g in range(Q):
                        copy_inter(dve.tensor_copy, q, g, inter_by_dve)
                place(i, v, 1)

            def split_input(i, v):
                dve.wait_ge(x_hi_made, i * 4 + v + 1)
                mine = slice((v % 2) * P, (v % 2 + 1) * P)
                dve.tensor_tensor(x_lo[:, :, mine], inter[:], x_hi[:, :, mine].bitcast(F32),
                                  ALU.subtract).then_inc(x_lo_made, 1)

            def step(now, prev):
                if now:
                    i, v = now[0], now[1] * 2
                    take_vectors(i, v)
                    if prev and items(*now):
                        compare(items(*now)[0][1])
                    if not prev:
                        for m in range(EARLY, X + 1):
                            compare(m)
                    place(i, v, 0)
                    take_products(i, v)
                    take_vectors(i, v + 1)
                    place(i, v, 2)
                    split_input(i, v)
                if prev:
                    dve.wait_ge(y_done, prev[0] * 2 + prev[1] + 1)
                    dve.tensor_copy(y_sb[:, bass.ds(prev[0] * 4 + prev[1] * 2, 2)],
                                    h1_ps[:, 0, 0:2]).then_inc(y_kept, 1)
                if now:
                    place(i, v + 1, 0)
                    if not prev:
                        split_weights()
                    take_products(i, v + 1)
                    split_input(i, v + 1)
                    place(i, v + 1, 2)

            passes(dve, step)
            dve.wait_ge(y_turned, 1)
            dve.tensor_copy(y_rows[:], h2_ps[0:B // P, 0, 0:P]).then_inc(y_ready, 1)


TABLES = [f"tbl_{f}" for f in range(26)]
INPUTS = ["r_dense_features", "ids", *TABLES, "W_top1", "b_top1", "W_top2", "b_top2", "W_top3"]


def lay_out_w1(w1):
    import numpy as np

    n, d, quadrants = 27, 128, 4
    places = -(-(n - 1) // quadrants)
    laid = np.zeros((128, places + 1, w1.shape[1]), w1.dtype)
    for i in range(n - 1):
        for j in range(i + 1, n):
            g, jj = divmod(j - 1, places)
            laid[32 * g + i, jj] = w1[d + i * n - i * (i + 1) // 2 + j - i - 1]
    laid[:, places] = w1[:d]
    return laid.reshape(128, -1)


def kernel(**inputs):
    import numpy as np
    import concourse.bacc as bacc
    from concourse.bass_utils import run_bass_kernel_spmd

    nc = bacc.Bacc("TRN2", target_bir_lowering=False, num_devices=1)
    given = {name: np.ascontiguousarray(inputs[name]) for name in INPUTS}
    given["W_top1_laid"] = lay_out_w1(given["W_top1"])
    arrays, aps = {}, {}
    for name, a in given.items():
        arrays[f"in_{name}"] = a
        aps[name] = nc.dram_tensor(f"in_{name}", a.shape, mybir.dt.from_np(a.dtype), kind="ExternalInput").ap()
    batch = aps["r_dense_features"].shape[0]
    out = nc.dram_tensor("out", (batch, 1), F32, kind="ExternalOutput").ap()
    dlrm_tower(nc, aps["r_dense_features"], aps["ids"], [aps[t] for t in TABLES], aps["W_top1"],
               aps["W_top1_laid"], aps["b_top1"], aps["W_top2"], aps["b_top2"], aps["W_top3"], out)
    r = run_bass_kernel_spmd(nc, [arrays], core_ids=[0])
    return r.results[0]["out"]
```

```python
from contextlib import ExitStack

import concourse.bass as bass
from concourse import mybir

P = 128
ALU = mybir.AluOpType
ACT = mybir.ActivationFunctionType
F32 = mybir.dt.float32
I32 = mybir.dt.int32
F16 = mybir.dt.float16
U32 = mybir.dt.uint32
F32R = mybir.dt.float32r
VECTORS = 27
SPREAD = (5, 6, 9, 14, 18, 24, 26)
ORDER = [f for f in range(VECTORS) if f not in SPREAD] + list(SPREAD)


def dlrm_tower(nc, dense, ids, tables, w1, w1_laid, b1, w2, b2, w3, out):
    B, D = dense.shape
    F = len(tables)
    N = F + 1
    H1, H2 = w1.shape[1], w2.shape[1]
    M1, M2 = H1 // P, H2 // P
    L2 = M1 * M2
    PAIRS = N * (N - 1) // 2
    R = 2 * P
    ROUNDS = B // R
    assert D == P and B % (2 * R) == 0 and w1.shape[0] == 2 * D + PAIRS and N == VECTORS
    PASSES = ROUNDS // 2

    Q = 4
    QS = P // Q
    COLS = 15
    JG = -(-COLS // Q)
    count = [min(JG, COLS - g * JG) for g in range(Q)]
    SECOND = 14
    merged = [(max(1, g * JG), min(12, g * JG + JG - 1) - max(1, g * JG) + 1) for g in range(Q)]
    HALF = QS // 2
    NA, ND = Q * Q + 1, Q * Q

    NR = N - len(SPREAD)
    groups = [list(range(a, min(a + 4, NR))) for a in range(0, NR, 4)]
    NG = len(groups)
    X = len(SPREAD)
    V = tables[SPREAD[0] - 1].shape[0]
    KT = 8
    KP = V // KT
    assert V == KP * KT and KP <= P and V <= 2048 and all(tables[f - 1].shape[0] == V for f in SPREAD)
    KH = KT // 2
    EARLY = X - 2
    IN_TILE, BEFORE_DOTS, AFTER_LAYER1, IN_TILE_2, AFTER_LAYER2, AFTER_LAYER3, LAST = [[k] for k in range(7)]
    BANKED = 6
    ITEM_AFTER = (2, 1)
    assert X == 7
    L1 = M1 // 2 * 3 * (JG + 1)

    with ExitStack() as ctx:
        def sb(name, shape, dt=F32):
            return ctx.enter_context(nc.sbuf_tensor(name, shape, dt))

        def ps(name, shape):
            return ctx.enter_context(nc.psum_tensor(name, shape, F32))

        def sem(name):
            return ctx.enter_context(nc.semaphore(name))

        ident = sb("ident", [P, P])
        ones = sb("ones", [P, P])
        idx = [sb(f"idx{v}", [P, F], I32) for v in range(4)]
        rows = [sb(f"rows{u}", [P, NR, D]) for u in range(2)]
        vecs = [sb(f"vecs{s}", [P, 2, P, N]) for s in range(2)]
        inter = sb("inter", [P, JG + 1, P])
        x_hi = sb("x_hi", [P, JG + 1, R], F32R)
        x_lo = sb("x_lo", [P, JG + 1, R], F32R)
        w_hi = sb("w_hi", [P, JG + 1, H1], F32R)
        w_lo = sb("w_lo", [P, JG + 1, H1], F32R)
        w2_sb = sb("w2_sb", [P, M1, H2])
        w3_sb = sb("w3_sb", [P, M2])
        b1_sb = sb("b1_sb", [P, M1])
        b2_sb = sb("b2_sb", [P, M2])
        h1_sb = sb("h1_sb", [P, M1, R])
        h2_sb = sb("h2_sb", [P, M2, R])
        y_sb = sb("y_sb", [P, B // P])
        y_rows = sb("y_rows", [B // P, P])
        ids_all = h1_sb[:, 0:2, :].rearrange("p m r -> p (m r)")[:, 0:B // P * F].bitcast(I32).rearrange(
            "p (t f) -> p t f", f=F)
        w_dense2 = sb("w_dense2", [P, H1])
        ids_f = w_dense2[:, 0:B // P * X].rearrange("p (t k) -> p t k", k=X)
        ids_t = sb("ids_t", [X, B], F16)
        pick_f = vecs[0][:].rearrange("p t b n -> p (t b n)")[0:X, 0:X * P].rearrange(
            "p (k q) -> p k q", q=P)
        pick = sb("pick", [X, X, P], F16)
        row_of_i = sb("row_of_i", [P, KT], I32)
        row_of = sb("row_of", [P, KT])
        t_hi = sb("t_hi", [P, X, KT, D], F32R)
        t_lo = sb("t_lo", [P, X, KT, D], F32R)
        mask_i = sb("mask_i", [P, JG], I32)
        mask_f = sb("mask_f", [P, JG])
        mask = sb("mask", [P, JG], I32)

        SIZE = KT * D
        WP = SIZE // H1
        W_PIECES = -(-(JG + 1) // WP)
        N_PIECES = X + W_PIECES
        IN_VECS = min(X, 2 * P * N // SIZE)
        assert SIZE % H1 == 0 and X <= IN_VECS + 1 and W_PIECES == 3 and (JG + 1) % WP == 1

        def places(n):
            return slice((n - X) * WP, min((n - X + 1) * WP, JG + 1))

        def piece(n, hi):
            if n < X:
                return (t_hi if hi else t_lo)[0:KP, n].rearrange("p t d -> p (t d)")
            return (w_hi if hi else w_lo)[:, places(n), :].rearrange("p j n -> p (j n)")

        def staged_piece(n):
            if n < IN_VECS:
                return vecs[1][:].rearrange("p t b n -> p (t b n)")[0:KP, n * SIZE:(n + 1) * SIZE]
            if n < X:
                return w2_sb[:].rearrange("p m n -> p (m n)")[0:KP]
            if n < N_PIECES - 1:
                return h1_sb[:].rearrange("p m r -> p (m r)")
            return h2_sb[:].rearrange("p m r -> p (m r)")

        onehot = [[sb(f"onehot{b}_{h}", [P, KH, R], F32R) for h in range(2)] for b in range(2)]

        vec_ps = [ps(f"vec_ps{k}", [P, 512]) for k in range(2)]
        dots_ps = ps("dots_ps", [P, 2, 512])
        h1_ps = ps("h1_ps", [P, M1 // 2, R])
        h2_ps = ps("h2_ps", [P, M2, R])
        ids_ps = ps("ids_ps", [P, 512])
        fetch_ps = ps("fetch_ps", [P, 512])

        ones_set = sem("ones_set")
        ident_made = sem("ident_made")
        picks_zero = sem("picks_zero")
        picks_made = sem("picks_made")
        picks_cast = sem("picks_cast")
        rows_counted = sem("rows_counted")
        rows_cast = sem("rows_cast")
        mask_begun = sem("mask_begun")
        mask_steps = sem("mask_steps")
        ids_in = sem("ids_in")
        ids_cast = sem("ids_cast")
        ids_turned = sem("ids_turned")
        ids_ready = sem("ids_ready")
        staged = [sem(f"staged{n}") for n in range(N_PIECES)]
        hi_made = sem("hi_made")
        lo_made = sem("lo_made")
        pads_zero = sem("pads_zero")
        dense_w_in = sem("dense_w_in")
        mlp_w_in = sem("mlp_w_in")
        dense_w_sum = sem("dense_w_sum")
        x_hi_made = sem("x_hi_made")
        x_lo_made = sem("x_lo_made")
        idx_in = [sem(f"idx_in{v}") for v in range(4)]
        dense_in = [sem(f"dense_in{u}") for u in range(2)]
        gathered = [[sem(f"gathered{u}_{k}") for k in range(NG)] for u in range(2)]
        groups_begun = sem("groups_begun")
        transposed = sem("transposed")
        vecs_by_act = sem("vecs_by_act")
        vecs_by_dve = sem("vecs_by_dve")
        ids_spread = sem("ids_spread")
        compared = sem("compared")
        onehot_used = sem("onehot_used")
        fetched = sem("fetched")
        dots_done = sem("dots_done")
        inter_by_act = sem("inter_by_act")
        inter_by_dve = sem("inter_by_dve")
        quadrants_begun = sem("quadrants_begun")
        h1_done = sem("h1_done")
        relu1_done = sem("relu1_done")
        h2_done = sem("h2_done")
        relu2_done = sem("relu2_done")
        y_done = sem("y_done")
        y_kept = sem("y_kept")
        y_turned = sem("y_turned")
        y_ready = sem("y_ready")
        out_written = sem("out_written")

        def groups_of(tiles):
            return (tiles + 2) * NG

        def item(i, r, k):
            return i * (2 * X) + (r + 1) * X + k, ((r + 1) * X + k) % 2

        def passes(eng, step, last_step):
            step((0, 0), None)
            with eng.Fori(0, PASSES - 1) as i:
                step((i, 1), (i, 0))
                step((i + 1, 0), (i, 1))
            last_step(PASSES - 1)

        def first_half(i, r):
            return 1 if isinstance(i, int) and i == PASSES - 1 and r == 1 else 0

        def y_at(i, r):
            return ids_ps[:, 0:2] if isinstance(i, int) and i == PASSES - 1 else h1_ps[:, 0, 0:2]

        def h1_half(half, spare):
            return fetch_ps[:].rearrange("p (m r) -> p m r", r=R) if spare and half else h1_ps

        def ids_at(m):
            if not isinstance(m, int) or m >= 2 * X:
                return ids_ps[:, 0:R]
            bank = (ids_ps[:], h1_ps[:].rearrange("p m r -> p (m r)"), h2_ps[:].rearrange("p m r -> p (m r)"),
                    dots_ps[:, 0, :] if m < X else ids_ps[:])[m % X // 2]
            return bank[:, m % X % 2 * R:(m % X % 2 + 1) * R]

        block = ctx.enter_context(nc.Block())

        @block.sync
        def _(sp):
            def load_idx(i, v):
                sp.dma_start(idx[v][:], ids[bass.ds(i * (4 * P) + v * P, P), :]).then_inc(idx_in[v], 16)

            def load_dense(i, v):
                u = v % 2
                sp.dma_start(rows[u][:, 0, :], dense[bass.ds(i * (4 * P) + v * P, P), :]).then_inc(dense_in[u], 16)

            load_idx(0, 0)
            sp.dma_start(ids_all, ids.rearrange("(t p) f -> p t f", p=P)).then_inc(ids_in, 16)
            for v in range(1, 4):
                load_idx(0, v)
            for v in range(2):
                load_dense(0, v)
            for n in range(N_PIECES):
                if n == X:
                    sp.wait_ge(ids_cast, X)
                    sp.wait_ge(ids_turned, 4)
                    sp.dma_start(w_dense2[:], w1[D + PAIRS:2 * D + PAIRS, :]).then_inc(dense_w_in, 16)
                if n == X + 1:
                    sp.wait_ge(hi_made, n)
                    sp.wait_ge(lo_made, n)
                if n < X:
                    src = tables[SPREAD[n] - 1].rearrange("(p t) d -> p (t d)", t=KT)
                else:
                    src = w1_laid[:, places(n).start * H1:places(n).stop * H1]
                sp.dma_start(staged_piece(n), src).then_inc(staged[n], 16)
                if n == X - 1:
                    with nc.allow_non_contiguous_dma(reason="a few hundred numbers, once"):
                        sp.dma_start(b1_sb[:], b1.rearrange("(m p) -> p m", p=P)).then_inc(mlp_w_in, 16)
                        sp.dma_start(b2_sb[:], b2.rearrange("(m p) -> p m", p=P)).then_inc(mlp_w_in, 16)
                        sp.dma_start(w3_sb[:], w3.rearrange("(m p) o -> p (m o)", p=P)).then_inc(mlp_w_in, 16)
                if n == X:
                    sp.wait_ge(hi_made, X)
                    sp.wait_ge(lo_made, X)
                    sp.dma_start(w2_sb[:], w2.rearrange("(m p) n -> p m n", p=P)).then_inc(mlp_w_in, 16)

            def refill(i, v, more):
                sp.wait_ge(transposed, i * (4 * NG) + groups_of(v + 1))
                load_dense(*((i, v + 2) if v < 2 else (i + 1, v - 2)))
                if more:
                    load_idx(i + 1, v)

            with sp.Fori(0, PASSES - 1) as i:
                for v in range(4):
                    refill(i, v, True)
            for v in range(2):
                refill(PASSES - 1, v, False)
            sp.wait_ge(y_ready, 1)
            sp.dma_start(out.rearrange("(t p) o -> t (p o)", p=P), y_rows[:]).then_inc(out_written, 16)
            sp.wait_ge(out_written, 16)

        @block.gpsimd
        def _(pool):
            def gather_tile(i, v):
                pool.wait_ge(idx_in[v], i * 16 + 16)
                for k, group in enumerate(groups):
                    pool.wait_ge(transposed, i * (4 * NG) + groups_of(v - 2) + k + 1)
                    pool.sem_inc(groups_begun, 1)
                    for s in group:
                        f = ORDER[s]
                        if f:
                            nc.gpsimd.indirect_dma_start(
                                out=rows[v % 2][:, s, :], out_offset=None, in_=tables[f - 1][:, :],
                                in_offset=bass.IndirectOffsetOnAxis(ap=idx[v][:, f - 1:f].bitcast(U32), axis=0),
                            ).then_inc(gathered[v % 2][k], 16)

            pool.iota(row_of_i[:], pattern=[[1, KT]], base=0, channel_multiplier=KT).then_inc(rows_counted, 1)
            pool.iota(mask_i[:], pattern=[[-1, JG]], base=0, channel_multiplier=1).then_inc(mask_begun, 1)
            pool.memset(ones[:], 1.0).then_inc(ones_set, 1)
            pool.memset(pick_f, 0.0).then_inc(picks_zero, 1)
            pool.wait_ge(ones_set, 1)
            pool.affine_select(out=ident[:], in_=ones[:], compare_op=ALU.is_equal, fill=0.0, base=0,
                               pattern=[[-1, P]], channel_multiplier=1).then_inc(ident_made, 1)
            pool.wait_ge(picks_zero, 1)
            pool.affine_select(out=pick_f, in_=pick_f, compare_op=ALU.not_equal, fill=1.0, base=0,
                               pattern=[[-1, X], [0, P]], channel_multiplier=1).then_inc(picks_made, 1)
            with pool.Fori(0, PASSES) as i:
                for v in range(4):
                    gather_tile(i, v)

        @block.tensor
        def _(pe):
            def transpose_rows(i, v, ks=range(NG), after=lambda k: None):
                u = v % 2
                for k in ks:
                    group = groups[k]
                    kk = v * NG + k
                    n_gathers = len([f for f in group if f])
                    pe.wait_ge(gathered[u][k], i * (32 * n_gathers) + (v // 2 + 1) * 16 * n_gathers)
                    if k == 0:
                        pe.wait_ge(dense_in[u], i * 32 + (v // 2 + 1) * 16)
                    freed = vecs_by_dve if kk % 2 else vecs_by_act
                    pe.wait_ge(freed, i * (2 * NG) + kk // 2 + 1)
                    for n, s in enumerate(group):
                        last = pe.transpose(vec_ps[kk % 2][:, n * P:(n + 1) * P], rows[u][:, s, :],
                                            ident[:])
                    last.then_inc(transposed, 1)
                    after(k)

            def dots(i, v):
                end = (v + 1) * NG
                vs = vecs[v // 2][:, v % 2]
                pe.wait_ge(vecs_by_act, i * (2 * NG) + (end + 1) // 2 + 1)
                pe.wait_ge(vecs_by_dve, i * (2 * NG) + end // 2 + 1)
                if v % 2 == 0:
                    pe.wait_ge(fetched, i * (2 * X) + (v // 2 + 1) * X)
                if not (isinstance(i, int) and i == 0 and v == 0):
                    pe.wait_ge(inter_by_act, i * (4 * NA) + v * NA)
                    pe.wait_ge(inter_by_dve, i * (4 * ND) + v * ND)
                for b in range(P):
                    q, n = b // QS, b % QS
                    o = (n % HALF) * N
                    last = pe.matmul(dots_ps[q * 32:q * 32 + N, n // HALF, o:o + N], vs[:, b, :],
                                     vs[:, b, :], start=True, stop=True)
                    if n == QS - 1:
                        last.then_inc(dots_done, 1)

            def spread_ids(round_, k, m=None):
                pe.matmul(ids_at(m), pick[:, k, :], ids_t[:, bass.ds(round_ * R, R)],
                          start=True, stop=True).then_inc(ids_spread, 1)

            def fetch(k, m, buf, for_round, halves=(0, 1)):
                for h in halves:
                    pe.wait_ge(compared, m * 2 + h + 1)
                    if h == 0 and not (isinstance(m, int) and m == 0):
                        pe.wait_ge(fetched, m)
                    first_rounds = isinstance(m, int) and m < 2 * X
                    spreads = h == 0 and k < X - 1 and not first_rounds
                    if spreads:
                        pe.wait_ge(compared, m * 2 + 2)
                    for t in range(KH):
                        for part in (t_hi, t_lo):
                            last = pe.matmul(fetch_ps[:, 0:R], part[0:KP, k, h * KH + t, :], onehot[buf][h][0:KP, t, :],
                                             start=(h == 0 and t == 0 and part is t_hi),
                                             stop=(h == 1 and t == KH - 1 and part is t_lo))
                            if spreads and t == 0 and part is t_hi:
                                spread_ids(for_round, k + 1)
                    last.then_inc(onehot_used, 1)
                    if h == 0 and first_rounds and m == X + 1:
                        pe.wait_ge(compared, m * 2 + 2)
                        for n in range(BANKED, X):
                            spread_ids(1, n, X + n)

            def fetch_items(i, r, ks, halves=(0, 1)):
                for k in ks:
                    fetch(k, *item(i, r, k), i * 2 + r + 1, halves)

            def layer1(i, r, half, some=range(L1)):
                spare = isinstance(i, int) and i == PASSES - 1
                tiles = i * 4 + (r + 1) * 2
                bank = h1_half(half, spare)
                for n in some:
                    m, at = divmod(n, 3 * (JG + 1))
                    c0 = (half * (M1 // 2) + m) * P
                    if n == 0 and half == first_half(i, r):
                        pe.wait_ge(lo_made, N_PIECES)
                        pe.wait_ge(mlp_w_in, 64)
                        pe.wait_ge(x_hi_made, tiles)
                    if n == 2 * (JG + 1) and half == first_half(i, r):
                        pe.wait_ge(x_lo_made, tiles)
                    if n == 0 and half == 0:
                        pe.wait_ge(y_kept, i * 2 + (1 if first_half(i, r) else r + 1))
                    elif n == 0 and spare:
                        pe.wait_ge(fetched, ROUNDS * X)
                    elif n == 0:
                        pe.wait_ge(relu1_done, i * (2 * M1) + r * M1 + M1 // 2)
                    if at < 2 * (JG + 1):
                        jj, w, x = at // 2, (w_hi, w_lo)[at % 2], x_hi
                    else:
                        jj, w, x = at - 2 * (JG + 1), w_hi, x_lo
                    last = pe.matmul(bank[:, m, :], w[:, jj, c0:c0 + P], x[:, jj, :],
                                     start=(at == 0), stop=(at == 3 * (JG + 1) - 1))
                    if n == L1 - 1:
                        last.then_inc(h1_done, 1)

            def layer2(i, r, some):
                for n in some:
                    m, k = n // M1, (n + first_half(i, r) * (M1 // 2)) % M1
                    if n == 0:
                        pe.wait_ge(relu1_done, i * (2 * M1) + r * M1 + M1 // 2)
                    if n == M1 // 2:
                        pe.wait_ge(relu1_done, i * (2 * M1) + (r + 1) * M1)
                    last = pe.matmul(h2_ps[:, m, :], w2_sb[:, k, m * P:(m + 1) * P],
                                     h1_sb[:, k, :], start=(n % M1 == 0), stop=(n % M1 == M1 - 1))
                    if n == L2 - 1:
                        last.then_inc(h2_done, 1)

            def layer3(i, r):
                pe.wait_ge(relu2_done, i * (2 * M2) + (r + 1) * M2)
                if first_half(i, r):
                    pe.wait_ge(y_kept, i * 2 + r + 1)
                y = y_at(i, r)
                for t in range(R // P):
                    for k in range(M2):
                        last = pe.matmul(y[:, t:t + 1], h2_sb[:, k, t * P:(t + 1) * P], w3_sb[:, k:k + 1],
                                         start=(k == 0), stop=(k == M2 - 1))
                last.then_inc(y_done, 1)

            pe.sem_inc(transposed, groups_of(0))
            pe.wait_ge(ident_made, 1)
            pe.wait_ge(ids_cast, X)
            for n, bank in enumerate((vec_ps[0], vec_ps[1], ids_ps, fetch_ps)):
                for t in range(4):
                    last = pe.transpose(bank[0:X, t * P:(t + 1) * P], ids_f[:, 4 * n + t, :], ident[:])
                last.then_inc(ids_turned, 1)
            pe.wait_ge(ids_ready, 4)
            pe.wait_ge(picks_cast, 1)

            def fetch_first(items_):
                for k in items_:
                    pe.wait_ge(hi_made, k + 1)
                    pe.wait_ge(lo_made, k + 1)
                    fetch(k, k, k % 2, 0)

            def shares(k, n):
                return range((k - 1) * n // (NG - 1), k * n // (NG - 1)) if k else range(0)

            def step(now, prev):
                i, r = now
                v = r * 2
                if prev:
                    spread_ids(i * 2 + r + 1, 0)

                    def with_layer1(k):
                        layer1(*prev, 0, shares(k, L1))
                        if k == ITEM_AFTER[0]:
                            fetch_items(i, r, IN_TILE)

                    def with_layer2(k):
                        layer2(*prev, shares(k, L2))
                        if k == ITEM_AFTER[1]:
                            fetch_items(i, r, IN_TILE_2)

                    transpose_rows(i, v, after=with_layer1)
                    fetch_items(i, r, BEFORE_DOTS)
                    dots(i, v)
                    layer1(*prev, 1)
                    fetch_items(i, r, AFTER_LAYER1)
                    transpose_rows(i, v + 1, after=with_layer2)
                    fetch_items(i, r, AFTER_LAYER2)
                    layer3(*prev)
                    fetch_items(i, r, AFTER_LAYER3)
                else:
                    for k in range(X):
                        spread_ids(0, k, k)
                    fetch_first(range(EARLY))
                    transpose_rows(i, v)
                    fetch_first(range(EARLY, X - 1))
                    for k in range(BANKED):
                        spread_ids(1, k, X + k)
                    fetch_first([X - 1])
                    dots(i, v)
                    fetch_items(i, r, [0, 1])
                    transpose_rows(i, v + 1)
                    fetch_items(i, r, range(2, X - 2))
                dots(i, v + 1)
                fetch_items(i, r, LAST if prev else [X - 2, X - 1])

            def last_step(i):
                transpose_rows(i, 2, after=lambda k: layer1(i, 0, 0, shares(k, L1)))
                dots(i, 2)
                transpose_rows(i, 3, range(NG - 1), after=lambda k: layer1(
                    i, 0, 1, range(min(k, NG - 2) * L1 // (NG - 2), min(k + 1, NG - 2) * L1 // (NG - 2))))
                layer2(i, 0, range(L2 // 2))
                transpose_rows(i, 3, [NG - 1])
                dots(i, 3)
                layer2(i, 0, range(L2 // 2, L2))
                layer1(i, 1, 1)
                layer3(i, 0)
                layer1(i, 1, 0)
                layer2(i, 1, range(L2))
                layer3(i, 1)

            passes(pe, step, last_step)
            pe.wait_ge(y_kept, ROUNDS + 1)
            pe.transpose(h2_ps[0:B // P, 0, 0:P], y_sb[:], ident[:]).then_inc(y_turned, 1)

        def copy_vecs(eng, copy, i, v, k, done):
            kk = v * NG + k
            a, n = groups[k][0], len(groups[k])
            eng.wait_ge(transposed, i * (4 * NG) + groups_of(0) + kk + 1)
            copy(vecs[v // 2][:, v % 2, :, a:a + n].rearrange("p b f -> p f b"),
                 vec_ps[kk % 2][:, 0:n * P].rearrange("p (f b) -> p f b", f=n)).then_inc(done, 1)

        def products_of(q, a, n):
            return dots_ps[q * 32:q * 32 + N, :, 0:HALF * N].rearrange(
                "p h (s j) -> p j h s", j=N)[:, a:a + n]

        def inter_of(q, g, a, n):
            return inter[g * 32:g * 32 + N, a:a + n, q * QS:(q + 1) * QS].rearrange("p j (h s) -> p j h s", h=2)

        @block.scalar
        def _(act):
            def copy_fetched(slot, k, m):
                act.wait_ge(onehot_used, m * 2 + 2)
                nc.scalar.copy(vecs[slot][:, :, :, NR + k],
                               fetch_ps[:, 0:R].rearrange("p (t b) -> p t b", t=2)).then_inc(fetched, 1)

            def copy_items(i, r, ks):
                for k in ks:
                    copy_fetched((r + 1) % 2, k, item(i, r, k)[0])

            act.sem_inc(vecs_by_act, 1)

            def split(n):
                act.wait_ge(staged[n], 16)
                if n == N_PIECES - 1:
                    act.wait_ge(dense_w_sum, 1)
                nc.scalar.copy(piece(n, True), staged_piece(n)).then_inc(hi_made, 1)

            for n in range(X):
                split(n)
                if n >= 2:
                    copy_fetched(0, n - 2, n - 2)
            assert X - 2 == EARLY

            def take_vectors(i, v, ks=range(NG)):
                for k in ks:
                    if (v * NG + k) % 2 == 0:
                        copy_vecs(act, nc.scalar.copy, i, v, k, vecs_by_act)

            def take_products(i, v):
                if not (isinstance(i, int) and i == 0 and v == 0):
                    act.wait_ge(x_lo_made, i * 4 + v)
                for q in range(Q):
                    act.wait_ge(dots_done, i * (4 * Q) + v * Q + q + 1)
                    for g in range(Q):
                        nc.scalar.copy(inter_of(q, g, 0, count[g]),
                                       products_of(q, g * JG, count[g])).then_inc(inter_by_act, 1)
                nc.scalar.copy(inter[:, JG, :], vecs[v // 2][:, v % 2, :, 0]).then_inc(inter_by_act, 1)

            def split_input(i, v):
                act.wait_ge(inter_by_act, i * (4 * NA) + (v + 1) * NA)
                act.wait_ge(inter_by_dve, i * (4 * ND) + (v + 1) * ND)
                nc.scalar.copy(x_hi[:, :, (v % 2) * P:(v % 2 + 1) * P], inter[:]).then_inc(x_hi_made, 1)

            def rectify(i, r, what):
                if what < 2:
                    act.wait_ge(mlp_w_in, 64)
                    act.wait_ge(h1_done, i * 4 + r * 2 + what + 1)
                    what = abs(what - first_half(i, r))
                    bank = h1_half(what, isinstance(i, int) and i == PASSES - 1)
                    for m in range(M1 // 2):
                        k = what * (M1 // 2) + m
                        nc.scalar.activation(h1_sb[:, k, :], bank[:, m, :], ACT.Relu,
                                             bias=b1_sb[:, k:k + 1]).then_inc(relu1_done, 1)
                else:
                    act.wait_ge(h2_done, i * 2 + r + 1)
                    for m in range(M2):
                        nc.scalar.activation(h2_sb[:, m, :], h2_ps[:, m, :], ACT.Relu,
                                             bias=b2_sb[:, m:m + 1]).then_inc(relu2_done, 1)

            def step(now, prev):
                i, r = now
                v = r * 2
                if prev:
                    take_vectors(i, v, range(ITEM_AFTER[0] + 1))
                    copy_items(i, r, IN_TILE)
                    take_vectors(i, v, range(ITEM_AFTER[0] + 1, NG))
                    rectify(*prev, 0)
                    copy_items(i, r, BEFORE_DOTS)
                else:
                    take_vectors(i, v)
                    for k in range(EARLY, X):
                        copy_fetched(0, k, k)
                    split(X)
                    act.wait_ge(lo_made, X)
                    act.wait_ge(pads_zero, 1)
                take_products(i, v)
                if prev:
                    rectify(*prev, 1)
                split_input(i, v)
                if prev:
                    copy_items(i, r, AFTER_LAYER1)
                    take_vectors(i, v + 1, range(ITEM_AFTER[1] + 1))
                    copy_items(i, r, IN_TILE_2)
                    take_vectors(i, v + 1, range(ITEM_AFTER[1] + 1, NG))
                    rectify(*prev, 2)
                else:
                    copy_items(i, r, [0, 1])
                    take_vectors(i, v + 1)
                    split(X + 1)
                copy_items(i, r, AFTER_LAYER2 + AFTER_LAYER3 if prev else range(2, X - 2))
                if not prev:
                    split(X + 2)
                take_products(i, v + 1)
                split_input(i, v + 1)
                copy_items(i, r, LAST if prev else [X - 2, X - 1])

            def last_step(i):
                take_vectors(i, 2)
                rectify(i, 0, 0)
                take_products(i, 2)
                take_vectors(i, 3, range(NG - 2))
                rectify(i, 0, 1)
                split_input(i, 2)
                take_vectors(i, 3, range(NG - 2, NG))
                take_products(i, 3)
                split_input(i, 3)
                rectify(i, 0, 2)
                for what in range(3):
                    rectify(i, 1, what)

            passes(act, step, last_step)

        @block.vector
        def _(dve):
            def compare(m, buf, halves=(0, 1)):
                for h in halves:
                    if h == 0:
                        dve.wait_ge(ids_spread, m // X * X + min(X, (m % X // 2 + 1) * 2)
                                    if isinstance(m, int) and m < 2 * X else m + 1)
                    if not (isinstance(m, int) and m < 2):
                        dve.wait_ge(onehot_used, m * 2 - 3 + h)
                    dve.tensor_tensor(
                        onehot[buf][h][0:KP],
                        ids_at(m)[0:KP].rearrange("p (o r) -> p o r", o=1).to_broadcast([KP, KH, R]),
                        row_of[0:KP, h * KH:(h + 1) * KH].rearrange("p (t o) -> p t o", o=1).to_broadcast([KP, KH, R]),
                        ALU.is_equal).then_inc(compared, 1)

            def compare_items(i, r, ks):
                for k in ks:
                    compare(*item(i, r, k))

            dve.sem_inc(vecs_by_dve, 1)
            dve.sem_inc(y_kept, 1)
            dve.wait_ge(ids_in, 16)
            for k, f in enumerate(SPREAD):
                dve.tensor_copy(ids_f[:, :, k], ids_all[:, :, f - 1]).then_inc(ids_cast, 1)
            dve.wait_ge(rows_counted, 1)
            dve.tensor_copy(row_of[:], row_of_i[:]).then_inc(rows_cast, 1)
            dve.wait_ge(picks_made, 1)
            dve.tensor_copy(pick[:], pick_f).then_inc(picks_cast, 1)
            for n, bank in enumerate((vec_ps[0], vec_ps[1], ids_ps, fetch_ps)):
                dve.wait_ge(ids_turned, n + 1)
                dve.tensor_copy(ids_t[:, n * 512:(n + 1) * 512], bank[0:X, :]).then_inc(ids_ready, 1)
            dve.wait_ge(rows_cast, 1)

            def split(n):
                dve.wait_ge(hi_made, n + 1)
                dve.tensor_tensor(piece(n, False), staged_piece(n), piece(n, True).bitcast(F32),
                                  ALU.subtract).then_inc(lo_made, 1)

            def make_mask():
                dve.wait_ge(mask_begun, 1)
                dve.tensor_copy(mask_f[:], mask_i[:]).then_inc(mask_steps, 1)
                dve.wait_ge(mask_steps, 1)
                for g in range(Q):
                    mine = slice(g * 32, (g + 1) * 32)
                    dve.tensor_scalar(mask_f[mine], mask_f[mine], -float(g * (32 + JG) + SECOND // 2), None,
                                      ALU.add).then_inc(mask_steps, 1)
                dve.wait_ge(mask_steps, Q + 1)
                dve.tensor_tensor(mask_f[:], mask_f[:], mask_f[:], ALU.mult).then_inc(mask_steps, 1)
                dve.wait_ge(mask_steps, Q + 2)
                dve.tensor_scalar(mask[:], mask_f[:], 40.0, None, ALU.is_gt).then_inc(mask_steps, 1)
                dve.wait_ge(mask_steps, Q + 3)
                dve.memset(inter[:], 0.0).then_inc(pads_zero, 1)

            for k in range(X):
                split(k)
                if k < EARLY:
                    compare(k, k % 2)
                if k == 1:
                    make_mask()

            def split_weights(pieces):
                for n in pieces:
                    if n == N_PIECES - 1:
                        dve.wait_ge(dense_w_in, 16)
                        dve.wait_ge(staged[n], 16)
                        dense_part = staged_piece(n)
                        dve.tensor_tensor(dense_part, dense_part, w_dense2[:], ALU.add).then_inc(dense_w_sum, 1)
                    split(n)

            def take_vectors(i, v, ks=range(NG)):
                for k in ks:
                    if (v * NG + k) % 2 == 1:
                        copy_vecs(dve, dve.tensor_copy, i, v, k, vecs_by_dve)

            def merge_products(i, v):
                for q in range(Q):
                    dve.wait_ge(inter_by_act, i * (4 * NA) + v * NA + (q + 1) * Q)
                    dve.sem_inc(quadrants_begun, 1)
                    for g, (c, n) in enumerate(merged):
                        a = c - g * JG
                        dve.copy_predicated(
                            inter_of(q, g, a, n),
                            mask[g * 32:g * 32 + N, a:a + n].rearrange("p (j h s) -> p j h s", h=1, s=1).to_broadcast(
                                [N, n, 2, HALF]),
                            products_of(q, c + SECOND, n)).then_inc(inter_by_dve, 1)

            def split_input(i, v):
                dve.wait_ge(x_hi_made, i * 4 + v + 1)
                mine = slice((v % 2) * P, (v % 2 + 1) * P)
                dve.tensor_tensor(x_lo[:, :, mine], inter[:], x_hi[:, :, mine].bitcast(F32),
                                  ALU.subtract).then_inc(x_lo_made, 1)

            def keep_y(i, r):
                dve.wait_ge(y_done, i * 2 + r + 1)
                dve.tensor_copy(y_sb[:, bass.ds(i * 4 + r * 2, 2)], y_at(i, r)).then_inc(y_kept, 1)

            def step(now, prev):
                i, r = now
                v = r * 2
                if prev:
                    compare(*item(i, r, 0), [0])
                    take_vectors(i, v, range(0, 2))
                    compare(*item(i, r, 0), [1])
                    compare_items(i, r, BEFORE_DOTS)
                    take_vectors(i, v, range(2, NG))
                    compare_items(i, r, AFTER_LAYER1)
                    merge_products(i, v)
                    compare_items(i, r, IN_TILE_2)
                    take_vectors(i, v + 1, range(0, 2))
                    compare_items(i, r, AFTER_LAYER2)
                    take_vectors(i, v + 1, range(2, NG))
                    compare_items(i, r, AFTER_LAYER3)
                    split_input(i, v)
                    keep_y(*prev)
                    compare_items(i, r, LAST)
                else:
                    take_vectors(i, v, range(0, 2))
                    compare(EARLY, EARLY % 2, [0])
                    take_vectors(i, v, range(2, NG))
                    compare(EARLY, EARLY % 2, [1])
                    for m in range(EARLY + 1, X + 2):
                        compare(m, m % 2)
                    split_weights([X])
                    merge_products(i, v)
                    compare_items(i, r, [2])
                    split_input(i, v)
                    take_vectors(i, v + 1, range(0, 1))
                    compare(*item(i, r, 3), [0])
                    take_vectors(i, v + 1, range(1, 3))
                    compare(*item(i, r, 3), [1])
                    take_vectors(i, v + 1, range(3, NG))
                    compare_items(i, r, range(4, X))
                    split_weights(range(X + 1, N_PIECES))
                merge_products(i, v + 1)
                split_input(i, v + 1)

            def last_step(i):
                take_vectors(i, 2)
                merge_products(i, 2)
                take_vectors(i, 3, range(NG - 1))
                split_input(i, 2)
                take_vectors(i, 3, [NG - 1])
                merge_products(i, 3)
                split_input(i, 3)
                keep_y(i, 0)
                keep_y(i, 1)

            passes(dve, step, last_step)
            dve.wait_ge(y_turned, 1)
            dve.tensor_copy(y_rows[:], h2_ps[0:B // P, 0, 0:P]).then_inc(y_ready, 1)


TABLES = [f"tbl_{f}" for f in range(26)]
INPUTS = ["r_dense_features", "ids", *TABLES, "W_top1", "b_top1", "W_top2", "b_top2", "W_top3"]


def columns_of_pairs():
    pairs = {}
    for c in range(15):
        for i in range(VECTORS):
            if 0 < (i - c) % VECTORS <= 13:
                pairs[i, c] = c
            elif 1 <= c <= 12 and i != c + 14:
                pairs[i, c] = c + 14
    assert len({frozenset(p) for p in ((i, j) for (i, _), j in pairs.items())}) == len(pairs) == 351
    return pairs


def lay_out_w1(w1):
    import numpy as np

    n, d = VECTORS, 128
    laid = np.zeros((128, 5, w1.shape[1]), w1.dtype)
    for (i, c), j in columns_of_pairs().items():
        g, jj = divmod(c, 4)
        a, b = sorted((ORDER[i], ORDER[j]))
        laid[32 * g + i, jj] = w1[d + a * n - a * (a + 1) // 2 + b - a - 1]
    laid[:, 4] = w1[:d]
    return laid.reshape(128, -1)


def kernel(**inputs):
    import numpy as np
    import concourse.bacc as bacc
    from concourse.bass_utils import run_bass_kernel_spmd

    nc = bacc.Bacc("TRN2", target_bir_lowering=False, num_devices=1)
    given = {name: np.ascontiguousarray(inputs[name]) for name in INPUTS}
    given["W_top1_laid"] = lay_out_w1(given["W_top1"])
    arrays, aps = {}, {}
    for name, a in given.items():
        arrays[f"in_{name}"] = a
        aps[name] = nc.dram_tensor(f"in_{name}", a.shape, mybir.dt.from_np(a.dtype), kind="ExternalInput").ap()
    batch = aps["r_dense_features"].shape[0]
    out = nc.dram_tensor("out", (batch, 1), F32, kind="ExternalOutput").ap()
    dlrm_tower(nc, aps["r_dense_features"], aps["ids"], [aps[t] for t in TABLES], aps["W_top1"],
               aps["W_top1_laid"], aps["b_top1"], aps["W_top2"], aps["b_top2"], aps["W_top3"], out)
    r = run_bass_kernel_spmd(nc, [arrays], core_ids=[0])
    return r.results[0]["out"]
```
